# Optimizing a Trainium2 kernel written in Bass

```python
import numpy as np
import jax
import jax.numpy as jnp

def _softmax(x, axis=-1):
    return jax.nn.softmax(x, axis=axis)

def _gelu(x):
    return jax.nn.gelu(x, approximate=True)

def _silu(x):
    return jax.nn.silu(x)

def _sigmoid(x):
    return jax.nn.sigmoid(x)

def _layernorm(x, axis=-1, eps=1e-05):
    m = jnp.mean(x, axis=axis, keepdims=True)
    v = jnp.var(x, axis=axis, keepdims=True)
    return (x - m) / jnp.sqrt(v + eps)

def _scatter_add(tgt, idx, src, axis=0):
    return tgt.at[idx].add(src)

def _segment_sum(src, seg, n):
    return jax.ops.segment_sum(src, seg, n)
kernel_name = 'mk_xattn_ffn_d2_seqx_r8_439ed5'

def setup_inputs(seed: int=0):
    np.random.seed(seed)
    _w = jnp.asarray

    def _rec_inputs():
        import jax
        import jax.numpy as jnp
        _rk = jax.random.key(seed)
        x = 7.22e-05 + 1 * jax.random.normal(jax.random.fold_in(_rk, 1), (16, 128, 256), jnp.float32)
        _lenS = 128 - jax.random.randint(jax.random.fold_in(_rk, 7), (16,), 0, max(1, 128 // 4) + 1, jnp.int32)
        _lenS2 = 128 - jax.random.randint(jax.random.fold_in(_rk, 8), (16,), 0, max(1, 128 // 4) + 1, jnp.int32)
        _ctx_2048P = jax.random.normal(jax.random.fold_in(_rk, 11), (16, 16, 256), jnp.float32)
        _ctx_2048c = jax.random.dirichlet(jax.random.fold_in(_rk, 511), 0.3 * jnp.ones((16,), jnp.float32), (16, 128))
        _ctx_2048t = jnp.einsum('bsk,bkd->bsd', _ctx_2048c, _ctx_2048P)
        _ctx_2048t = _ctx_2048t * jax.lax.rsqrt(jnp.mean(jnp.square(_ctx_2048t)) + 1e-12) * 0.953939
        ctx_2048 = 4.13588e-05 + 0.999923 * (_ctx_2048t + 0.3 * jax.random.normal(jax.random.fold_in(_rk, 611), (16, 128, 256), jnp.float32))
        return (x, ctx_2048)
    x, ctx_2048 = _rec_inputs()

    def _L0_xattn_setup():
        import jax, jax.numpy as jnp
        import numpy as np
        N_HEAD = 8
        key = jax.random.key(seed)
        k1, k2, k3 = jax.random.split(key, 3)
        B, D, L = (4, 128, 256)
        q = jax.random.normal(k1, (B, D, L), dtype=jnp.float32)
        k = jax.random.normal(k2, (B, D, L), dtype=jnp.float32)
        v = jax.random.normal(k3, (B, D, L), dtype=jnp.float32)
        gamma = jnp.ones((), dtype=jnp.float32)
        return {'q': q, 'k': k, 'v': v, 'gamma': gamma}
    _L0_xattn_all = _L0_xattn_setup()
    _L0_xattn_in = {k: v for k, v in _L0_xattn_all.items() if k in ('gamma',)}
    del _L0_xattn_all

    def _L0_ffn_setup():
        import jax, jax.numpy as jnp
        import numpy as np
        ALPHA = 1.702
        LIMIT = 7.0
        TOP_K = 4
        B, S, H = (1, 128, 256)
        E, D = (16, 256)
        key = jax.random.key(seed)
        ks = jax.random.split(key, 7)
        s = 0.02
        return {'hidden_states': jax.random.normal(ks[0], (B, S, H), dtype=jnp.float32), 'router_weight': jax.random.normal(ks[1], (E, H), dtype=jnp.float32) * s, 'router_bias': jax.random.normal(ks[2], (E,), dtype=jnp.float32) * s, 'gate_up_proj': jax.random.normal(ks[3], (E, H, 2 * D), dtype=jnp.float32) * s, 'gate_up_proj_bias': jax.random.normal(ks[4], (E, 2 * D), dtype=jnp.float32) * s, 'down_proj': jax.random.normal(ks[5], (E, D, H), dtype=jnp.float32) * s, 'down_proj_bias': jax.random.normal(ks[6], (E, H), dtype=jnp.float32) * s}
    _L0_ffn_all = _L0_ffn_setup()
    _L0_ffn_in = {k: v for k, v in _L0_ffn_all.items() if k in ('router_weight', 'router_bias', 'gate_up_proj', 'gate_up_proj_bias', 'down_proj', 'down_proj_bias')}
    del _L0_ffn_all

    def _L1_xattn_setup():
        import jax, jax.numpy as jnp
        import numpy as np
        FP8_MAX = 448.0
        EPS = 1e-05

        def _fp8_roundtrip(x):
            return x.astype(jnp.float8_e4m3fn).astype(jnp.float32)

        def _div_clamp_fp8(x, scale):
            y = jnp.clip(x.astype(jnp.float32) / scale, -FP8_MAX, FP8_MAX)
            y = y.astype(jnp.bfloat16).astype(jnp.float32)
            return _fp8_roundtrip(y)

        def _ln(x, w, b):
            mu = jnp.mean(x, axis=-1, keepdims=True)
            var = jnp.mean(jnp.square(x - mu), axis=-1, keepdims=True)
            return (x - mu) * jax.lax.rsqrt(var + EPS) * w + b

        def _fp8_linear_pertensor(x, wq, w_scale, in_scale):
            xq = _div_clamp_fp8(x, in_scale)
            return jnp.einsum('bsi,oi->bso', xq * in_scale, wq) * w_scale

        def _gqa(q, k, v):
            scale = 1.0 / np.sqrt(q.shape[-1])
            scores = jnp.einsum('bsghd,btgd->bghst', q, k) * scale
            p = jax.nn.softmax(scores, axis=-1)
            return jnp.einsum('bghst,btgd->bsghd', p, v)
        key = jax.random.key(seed)
        ks = jax.random.split(key, 8)
        B, S, SC, H, NH, G, D = (2, 256, 64, 256, 16, 8, 128)

        def qw(k, out_f, in_f):
            w = jax.random.normal(k, (out_f, in_f), jnp.float32) * 0.02
            sc = jnp.max(jnp.abs(w)) / FP8_MAX
            return (_fp8_roundtrip(w / sc), sc.astype(jnp.float32))
        wq, wq_s = qw(ks[0], NH * D, H)
        wqx, wqx_s = qw(ks[1], NH * D, H)
        wk, wk_s = qw(ks[2], G * D, H)
        wv, wv_s = qw(ks[3], G * D, H)
        wproj, wp_s = qw(ks[4], H, 2 * NH * D)
        return {'hidden_states': jax.random.normal(ks[5], (B, S, H), jnp.float32), 'cond': jax.random.normal(ks[6], (B, SC, H), jnp.float32), 'ln_w': jnp.ones((H,), jnp.float32), 'ln_b': jnp.zeros((H,), jnp.float32), 'wq': wq, 'wq_scale': wq_s, 'q_in_scale': jnp.full((H,), 0.05, jnp.float32), 'wqx': wqx, 'wqx_scale': wqx_s, 'qx_in_scale': jnp.full((H,), 0.05, jnp.float32), 'wk': wk, 'wk_scale': wk_s, 'k_in_scale': jnp.full((H,), 0.05, jnp.float32), 'wv': wv, 'wv_scale': wv_s, 'v_in_scale': jnp.full((H,), 0.05, jnp.float32), 'w_kv_x': jax.random.normal(ks[7], (2 * G * D, H), jnp.float32) * 0.02, 'qln_w': jnp.ones((D,), jnp.float32), 'qln_b': jnp.zeros((D,), jnp.float32), 'kln_w': jnp.ones((D,), jnp.float32), 'kln_b': jnp.zeros((D,), jnp.float32), 'qxln_w': jnp.ones((D,), jnp.float32), 'qxln_b': jnp.zeros((D,), jnp.float32), 'kxln_w': jnp.ones((D,), jnp.float32), 'kxln_b': jnp.zeros((D,), jnp.float32), 'wproj': wproj, 'proj_w_scale': wp_s, 'proj_in_scale': jnp.asarray(0.05, jnp.float32), 'proj_smooth': jnp.full((2 * NH * D,), 0.05, jnp.float32)}
    _L1_xattn_all = _L1_xattn_setup()
    _L1_xattn_in = {k: v for k, v in _L1_xattn_all.items() if k in ('ln_w', 'ln_b', 'wq', 'wq_scale', 'q_in_scale', 'wqx', 'wqx_scale', 'qx_in_scale', 'wk', 'wk_scale', 'k_in_scale', 'wv', 'wv_scale', 'v_in_scale', 'w_kv_x', 'qln_w', 'qln_b', 'kln_w', 'kln_b', 'qxln_w', 'qxln_b', 'kxln_w', 'kxln_b', 'wproj', 'proj_w_scale', 'proj_in_scale', 'proj_smooth')}
    del _L1_xattn_all

    def _L1_ffn_setup():
        import jax, jax.numpy as jnp
        import numpy as np
        B, S, D = (2, 256, 256)
        H, KV, HD = (16, 4, 128)
        E, F, TOPK = (8, 512, 2)
        THETA = 1000000.0
        EPS = 1e-05

        def rmsnorm(x, w):
            var = jnp.mean(jnp.square(x), axis=-1, keepdims=True)
            return x * jax.lax.rsqrt(var + EPS) * w

        def rope_cos_sin(seq_len):
            inv_freq = 1.0 / THETA ** (jnp.arange(0, HD, 2, dtype=jnp.float32) / HD)
            ang = jnp.arange(seq_len, dtype=jnp.float32)[:, None] * inv_freq[None, :]
            return (jnp.cos(ang)[None, :, None, :], jnp.sin(ang)[None, :, None, :])

        def apply_rope(x, cos, sin):
            x1, x2 = jnp.split(x, 2, axis=-1)
            return jnp.concatenate([x1 * cos - x2 * sin, x2 * cos + x1 * sin], axis=-1)

        def attention(x, wq, wk, wv, wo):
            b, s, _ = x.shape
            q = (x @ wq).reshape(b, s, H, HD)
            k = (x @ wk).reshape(b, s, KV, HD)
            v = (x @ wv).reshape(b, s, KV, HD)
            cos, sin = rope_cos_sin(s)
            q = apply_rope(q, cos, sin)
            k = apply_rope(k, cos, sin)
            rep = H // KV
            k = jnp.repeat(k, rep, axis=2)
            v = jnp.repeat(v, rep, axis=2)
            scores = jnp.einsum('bqhd,bkhd->bhqk', q, k) / np.sqrt(HD)
            causal = jnp.tril(jnp.ones((s, s), dtype=bool))
            scores = jnp.where(causal[None, None], scores, jnp.finfo(scores.dtype).min)
            probs = jax.nn.softmax(scores, axis=-1)
            out = jnp.einsum('bhqk,bkhd->bqhd', probs, v).reshape(b, s, H * HD)
            return out @ wo

        def moe(x, gate_w, w1, w3, w2):
            b, s, d = x.shape
            xt = x.reshape(b * s, d)
            logits = xt @ gate_w
            topv, topi = jax.lax.top_k(logits, TOPK)
            probs = jax.nn.softmax(topv, axis=-1)
            w = jnp.zeros_like(logits)
            for kk in range(TOPK):
                w = w + jax.nn.one_hot(topi[:, kk], E, dtype=logits.dtype) * probs[:, kk:kk + 1]
            out = jnp.zeros_like(xt)
            for e in range(E):
                h = jax.nn.silu(xt @ w1[e]) * (xt @ w3[e])
                out = out + w[:, e:e + 1] * (h @ w2[e])
            return out.reshape(b, s, d)
        key = jax.random.key(seed)
        ks = jax.random.split(key, 10)
        init = lambda k, shape: jax.random.normal(k, shape, jnp.float32) * 0.02
        return {'hidden_states': jax.random.normal(ks[0], (B, S, D), jnp.float32), 'norm1_w': jnp.ones((D,), jnp.float32), 'norm2_w': jnp.ones((D,), jnp.float32), 'wq': init(ks[1], (D, H * HD)), 'wk': init(ks[2], (D, KV * HD)), 'wv': init(ks[3], (D, KV * HD)), 'wo': init(ks[4], (H * HD, D)), 'gate_w': init(ks[5], (D, E)), 'w1': init(ks[6], (E, D, F)), 'w3': init(ks[7], (E, D, F)), 'w2': init(ks[8], (E, F, D))}
    _L1_ffn_all = _L1_ffn_setup()
    _L1_ffn_in = {k: v for k, v in _L1_ffn_all.items() if k in ('norm1_w', 'norm2_w', 'wq', 'wk', 'wv', 'wo', 'gate_w', 'w1', 'w3', 'w2')}
    del _L1_ffn_all
    return {'x': x, 'ctx_2048': ctx_2048, 'L0_xattn_gamma': _L0_xattn_in['gamma'], 'L0_ffn_router_weight': _L0_ffn_in['router_weight'], 'L0_ffn_router_bias': _L0_ffn_in['router_bias'], 'L0_ffn_gate_up_proj': _L0_ffn_in['gate_up_proj'], 'L0_ffn_gate_up_proj_bias': _L0_ffn_in['gate_up_proj_bias'], 'L0_ffn_down_proj': _L0_ffn_in['down_proj'], 'L0_ffn_down_proj_bias': _L0_ffn_in['down_proj_bias'], 'L1_xattn_ln_w': _L1_xattn_in['ln_w'], 'L1_xattn_ln_b': _L1_xattn_in['ln_b'], 'L1_xattn_wq': _L1_xattn_in['wq'], 'L1_xattn_wq_scale': _L1_xattn_in['wq_scale'], 'L1_xattn_q_in_scale': _L1_xattn_in['q_in_scale'], 'L1_xattn_wqx': _L1_xattn_in['wqx'], 'L1_xattn_wqx_scale': _L1_xattn_in['wqx_scale'], 'L1_xattn_qx_in_scale': _L1_xattn_in['qx_in_scale'], 'L1_xattn_wk': _L1_xattn_in['wk'], 'L1_xattn_wk_scale': _L1_xattn_in['wk_scale'], 'L1_xattn_k_in_scale': _L1_xattn_in['k_in_scale'], 'L1_xattn_wv': _L1_xattn_in['wv'], 'L1_xattn_wv_scale': _L1_xattn_in['wv_scale'], 'L1_xattn_v_in_scale': _L1_xattn_in['v_in_scale'], 'L1_xattn_w_kv_x': _L1_xattn_in['w_kv_x'], 'L1_xattn_qln_w': _L1_xattn_in['qln_w'], 'L1_xattn_qln_b': _L1_xattn_in['qln_b'], 'L1_xattn_kln_w': _L1_xattn_in['kln_w'], 'L1_xattn_kln_b': _L1_xattn_in['kln_b'], 'L1_xattn_qxln_w': _L1_xattn_in['qxln_w'], 'L1_xattn_qxln_b': _L1_xattn_in['qxln_b'], 'L1_xattn_kxln_w': _L1_xattn_in['kxln_w'], 'L1_xattn_kxln_b': _L1_xattn_in['kxln_b'], 'L1_xattn_wproj': _L1_xattn_in['wproj'], 'L1_xattn_proj_w_scale': _L1_xattn_in['proj_w_scale'], 'L1_xattn_proj_in_scale': _L1_xattn_in['proj_in_scale'], 'L1_xattn_proj_smooth': _L1_xattn_in['proj_smooth'], 'L1_ffn_norm1_w': _L1_ffn_in['norm1_w'], 'L1_ffn_norm2_w': _L1_ffn_in['norm2_w'], 'L1_ffn_wq': _L1_ffn_in['wq'], 'L1_ffn_wk': _L1_ffn_in['wk'], 'L1_ffn_wv': _L1_ffn_in['wv'], 'L1_ffn_wo': _L1_ffn_in['wo'], 'L1_ffn_gate_w': _L1_ffn_in['gate_w'], 'L1_ffn_w1': _L1_ffn_in['w1'], 'L1_ffn_w3': _L1_ffn_in['w3'], 'L1_ffn_w2': _L1_ffn_in['w2']}

def reference(x, ctx_2048, L0_xattn_gamma, L0_ffn_router_weight, L0_ffn_router_bias, L0_ffn_gate_up_proj, L0_ffn_gate_up_proj_bias, L0_ffn_down_proj, L0_ffn_down_proj_bias, L1_xattn_ln_w, L1_xattn_ln_b, L1_xattn_wq, L1_xattn_wq_scale, L1_xattn_q_in_scale, L1_xattn_wqx, L1_xattn_wqx_scale, L1_xattn_qx_in_scale, L1_xattn_wk, L1_xattn_wk_scale, L1_xattn_k_in_scale, L1_xattn_wv, L1_xattn_wv_scale, L1_xattn_v_in_scale, L1_xattn_w_kv_x, L1_xattn_qln_w, L1_xattn_qln_b, L1_xattn_kln_w, L1_xattn_kln_b, L1_xattn_qxln_w, L1_xattn_qxln_b, L1_xattn_kxln_w, L1_xattn_kxln_b, L1_xattn_wproj, L1_xattn_proj_w_scale, L1_xattn_proj_in_scale, L1_xattn_proj_smooth, L1_ffn_norm1_w, L1_ffn_norm2_w, L1_ffn_wq, L1_ffn_wk, L1_ffn_wv, L1_ffn_wo, L1_ffn_gate_w, L1_ffn_w1, L1_ffn_w3, L1_ffn_w2):
    import jax
    import jax.numpy as jnp

    def _L0_xattn_ref(q, k, v, gamma):
        import jax, jax.numpy as jnp
        import numpy as np
        N_HEAD = 8
        B, Dq, Lq = q.shape
        Dv, Lk = (v.shape[-2], v.shape[-1])
        h = N_HEAD
        dq = Dq // h
        dv = Dv // h
        qh = q.reshape(B, h, dq, Lq)
        kh = k.reshape(B, h, dq, Lk)
        vh = v.reshape(B, h, dv, Lk)
        scale = 1.0 / jnp.sqrt(jnp.asarray(dq, dtype=q.dtype))
        qk = jnp.einsum('bhdq,bhdl->bhql', qh, kh) * scale
        sm = jax.nn.softmax(qk, axis=-1)
        ret = jnp.einsum('bhql,bhdl->bhdq', sm, vh)
        ret = ret.reshape(B, Dv, Lq)
        return gamma * ret

    def _L0_ffn_ref(hidden_states, router_weight, router_bias, gate_up_proj, gate_up_proj_bias, down_proj, down_proj_bias):
        import jax, jax.numpy as jnp
        import numpy as np
        ALPHA = 1.702
        LIMIT = 7.0
        TOP_K = 4
        B, S, H = (1, 128, 256)
        E, D = (16, 256)
        batch, seq, hdim = hidden_states.shape
        x = hidden_states.reshape(-1, hdim)
        T = x.shape[0]
        logits = x @ router_weight.T + router_bias
        top_val, top_idx = jax.lax.top_k(logits, TOP_K)
        top_val = jax.nn.softmax(top_val, axis=-1)
        router_scores = jnp.zeros_like(logits).at[jnp.arange(T)[:, None], top_idx].set(top_val)
        gate_up = jnp.einsum('th,ehd->etd', x, gate_up_proj) + gate_up_proj_bias[:, None, :]
        gate = gate_up[..., ::2]
        up = gate_up[..., 1::2]
        gate = jnp.minimum(gate, LIMIT)
        up = jnp.clip(up, -LIMIT, LIMIT)
        glu = gate * jax.nn.sigmoid(gate * ALPHA)
        out = jnp.einsum('etd,edh->eth', (up + 1.0) * glu, down_proj) + down_proj_bias[:, None, :]
        out = out * router_scores.T[:, :, None]
        out = out.sum(axis=0)
        return out.reshape(batch, seq, hdim)

    def _L1_xattn_ref(hidden_states, cond, ln_w, ln_b, wq, wq_scale, q_in_scale, wqx, wqx_scale, qx_in_scale, wk, wk_scale, k_in_scale, wv, wv_scale, v_in_scale, w_kv_x, qln_w, qln_b, kln_w, kln_b, qxln_w, qxln_b, kxln_w, kxln_b, wproj, proj_w_scale, proj_in_scale, proj_smooth):
        import jax, jax.numpy as jnp
        import numpy as np
        FP8_MAX = 448.0
        EPS = 1e-05

        def _fp8_roundtrip(x):
            return x.astype(jnp.float8_e4m3fn).astype(jnp.float32)

        def _div_clamp_fp8(x, scale):
            y = jnp.clip(x.astype(jnp.float32) / scale, -FP8_MAX, FP8_MAX)
            y = y.astype(jnp.bfloat16).astype(jnp.float32)
            return _fp8_roundtrip(y)

        def _ln(x, w, b):
            mu = jnp.mean(x, axis=-1, keepdims=True)
            var = jnp.mean(jnp.square(x - mu), axis=-1, keepdims=True)
            return (x - mu) * jax.lax.rsqrt(var + EPS) * w + b

        def _fp8_linear_pertensor(x, wq, w_scale, in_scale):
            xq = _div_clamp_fp8(x, in_scale)
            return jnp.einsum('bsi,oi->bso', xq * in_scale, wq) * w_scale

        def _gqa(q, k, v):
            scale = 1.0 / np.sqrt(q.shape[-1])
            scores = jnp.einsum('bsghd,btgd->bghst', q, k) * scale
            p = jax.nn.softmax(scores, axis=-1)
            return jnp.einsum('bghst,btgd->bsghd', p, v)
        b, s, _ = hidden_states.shape
        sc = cond.shape[1]
        d = qln_w.shape[0]
        nh = wq.shape[0] // d
        g = wk.shape[0] // d
        hpg = nh // g
        ln_out = _ln(hidden_states, ln_w, ln_b)
        q = _fp8_linear_pertensor(ln_out, wq, wq_scale, q_in_scale).reshape(b, s, g, hpg, d)
        q = _ln(q, qln_w, qln_b)
        k = _fp8_linear_pertensor(ln_out, wk, wk_scale, k_in_scale).reshape(b, s, g, d)
        k = _ln(k, kln_w, kln_b)
        v = _fp8_linear_pertensor(ln_out, wv, wv_scale, v_in_scale).reshape(b, s, g, d)
        core = _gqa(q, k, v).reshape(b, s, nh * d)
        qx = _fp8_linear_pertensor(ln_out, wqx, wqx_scale, qx_in_scale).reshape(b, s, g, hpg, d)
        qx = _ln(qx, qxln_w, qxln_b)
        kvx = jnp.einsum('bsi,oi->bso', cond, w_kv_x)
        kx, vx = jnp.split(kvx, 2, axis=-1)
        kx = _ln(kx.reshape(b, sc, g, d), kxln_w, kxln_b)
        vx = vx.reshape(b, sc, g, d)
        xout = _gqa(qx, kx, vx).reshape(b, s, nh * d)
        cat = jnp.concatenate([core, xout], axis=-1)
        catq = _div_clamp_fp8(cat, proj_smooth)
        return jnp.einsum('bsi,oi->bso', catq, wproj) * (proj_in_scale * proj_w_scale)

    def _L1_ffn_ref(hidden_states, norm1_w, norm2_w, wq, wk, wv, wo, gate_w, w1, w3, w2):
        import jax, jax.numpy as jnp
        import numpy as np
        B, S, D = (2, 256, 256)
        H, KV, HD = (16, 4, 128)
        E, F, TOPK = (8, 512, 2)
        THETA = 1000000.0
        EPS = 1e-05

        def rmsnorm(x, w):
            var = jnp.mean(jnp.square(x), axis=-1, keepdims=True)
            return x * jax.lax.rsqrt(var + EPS) * w

        def rope_cos_sin(seq_len):
            inv_freq = 1.0 / THETA ** (jnp.arange(0, HD, 2, dtype=jnp.float32) / HD)
            ang = jnp.arange(seq_len, dtype=jnp.float32)[:, None] * inv_freq[None, :]
            return (jnp.cos(ang)[None, :, None, :], jnp.sin(ang)[None, :, None, :])

        def apply_rope(x, cos, sin):
            x1, x2 = jnp.split(x, 2, axis=-1)
            return jnp.concatenate([x1 * cos - x2 * sin, x2 * cos + x1 * sin], axis=-1)

        def attention(x, wq, wk, wv, wo):
            b, s, _ = x.shape
            q = (x @ wq).reshape(b, s, H, HD)
            k = (x @ wk).reshape(b, s, KV, HD)
            v = (x @ wv).reshape(b, s, KV, HD)
            cos, sin = rope_cos_sin(s)
            q = apply_rope(q, cos, sin)
            k = apply_rope(k, cos, sin)
            rep = H // KV
            k = jnp.repeat(k, rep, axis=2)
            v = jnp.repeat(v, rep, axis=2)
            scores = jnp.einsum('bqhd,bkhd->bhqk', q, k) / np.sqrt(HD)
            causal = jnp.tril(jnp.ones((s, s), dtype=bool))
            scores = jnp.where(causal[None, None], scores, jnp.finfo(scores.dtype).min)
            probs = jax.nn.softmax(scores, axis=-1)
            out = jnp.einsum('bhqk,bkhd->bqhd', probs, v).reshape(b, s, H * HD)
            return out @ wo

        def moe(x, gate_w, w1, w3, w2):
            b, s, d = x.shape
            xt = x.reshape(b * s, d)
            logits = xt @ gate_w
            topv, topi = jax.lax.top_k(logits, TOPK)
            probs = jax.nn.softmax(topv, axis=-1)
            w = jnp.zeros_like(logits)
            for kk in range(TOPK):
                w = w + jax.nn.one_hot(topi[:, kk], E, dtype=logits.dtype) * probs[:, kk:kk + 1]
            out = jnp.zeros_like(xt)
            for e in range(E):
                h = jax.nn.silu(xt @ w1[e]) * (xt @ w3[e])
                out = out + w[:, e:e + 1] * (h @ w2[e])
            return out.reshape(b, s, d)
        attn_out = attention(rmsnorm(hidden_states, norm1_w), wq, wk, wv, wo)
        h = hidden_states + attn_out
        out = h + moe(rmsnorm(h, norm2_w), gate_w, w1, w3, w2)
        return out
    x = x + _L0_xattn_ref(_layernorm(x, axis=-1), ctx_2048, ctx_2048, L0_xattn_gamma)
    x = x + _L0_ffn_ref(_layernorm(x, axis=-1), L0_ffn_router_weight, L0_ffn_router_bias, L0_ffn_gate_up_proj, L0_ffn_gate_up_proj_bias, L0_ffn_down_proj, L0_ffn_down_proj_bias)
    x = x + _L1_xattn_ref(_layernorm(x, axis=-1), ctx_2048, L1_xattn_ln_w, L1_xattn_ln_b, L1_xattn_wq, L1_xattn_wq_scale, L1_xattn_q_in_scale, L1_xattn_wqx, L1_xattn_wqx_scale, L1_xattn_qx_in_scale, L1_xattn_wk, L1_xattn_wk_scale, L1_xattn_k_in_scale, L1_xattn_wv, L1_xattn_wv_scale, L1_xattn_v_in_scale, L1_xattn_w_kv_x, L1_xattn_qln_w, L1_xattn_qln_b, L1_xattn_kln_w, L1_xattn_kln_b, L1_xattn_qxln_w, L1_xattn_qxln_b, L1_xattn_kxln_w, L1_xattn_kxln_b, L1_xattn_wproj, L1_xattn_proj_w_scale, L1_xattn_proj_in_scale, L1_xattn_proj_smooth)
    x = x + _L1_ffn_ref(_layernorm(x, axis=-1), L1_ffn_norm1_w, L1_ffn_norm2_w, L1_ffn_wq, L1_ffn_wk, L1_ffn_wv, L1_ffn_wo, L1_ffn_gate_w, L1_ffn_w1, L1_ffn_w3, L1_ffn_w2)
    return x

_drawn_inputs = setup_inputs


def setup_inputs(seed=0):
    import zlib

    import numpy as np

    out = dict(_drawn_inputs(seed))
    spreads = {'L1_xattn_ln_w': (1.0, 0.6),
     'L1_xattn_ln_b': (0.0, 0.326),
     'L1_xattn_q_in_scale': (0.05000000074505806, 0.6),
     'L1_xattn_qx_in_scale': (0.05000000074505806, 0.6),
     'L1_xattn_k_in_scale': (0.05000000074505806, 0.6),
     'L1_xattn_v_in_scale': (0.05000000074505806, 0.6),
     'L1_xattn_qln_w': (1.0, 0.6),
     'L1_xattn_qln_b': (0.0, 0.8),
     'L1_xattn_kln_w': (1.0, 0.6),
     'L1_xattn_kln_b': (0.0, 0.8),
     'L1_xattn_qxln_w': (1.0, 0.6),
     'L1_xattn_qxln_b': (0.0, 0.8),
     'L1_xattn_kxln_w': (1.0, 0.6),
     'L1_xattn_kxln_b': (0.0, 0.8),
     'L1_xattn_proj_smooth': (0.05000000074505806, 0.566),
     'L1_ffn_norm1_w': (1.0, 0.6),
     'L1_ffn_norm2_w': (1.0, 0.6)}
    factors = {'L0_ffn_router_bias': 8.0,
     'L0_ffn_gate_up_proj_bias': 8.0,
     'L0_ffn_down_proj_bias': 6.708,
     'L1_ffn_wq': 8.0,
     'L1_ffn_wk': 8.0,
     'L1_ffn_gate_w': 7.89,
     'L1_ffn_w1': 7.076,
     'L1_ffn_w3': 7.01,
     'L1_ffn_w2': 7.0}
    for name, (base, spread) in spreads.items():
        noise = np.random.default_rng([zlib.crc32(name.encode()), seed]).standard_normal(out[name].shape)
        drawn = base * np.exp(spread * noise) if base else spread * noise
        out[name] = jnp.asarray(drawn.astype(out[name].dtype))
    for name, factor in factors.items():
        out[name] = (out[name] * factor).astype(out[name].dtype)
    return out
```

```python
from contextlib import ExitStack

import numpy as np

import concourse.bass as bass
from concourse import mybir

P = 128
B = 16
D = 256
DC = D // P
T = B * P
EPS = 1e-5
GRP = 4
NG = B // GRP
BANK = 512
BIG = 3.0e38

ALU = mybir.AluOpType
ACT = mybir.ActivationFunctionType
AX = mybir.AxisListType
F32 = mybir.dt.float32
BF16 = mybir.dt.bfloat16
F16 = mybir.dt.float16
U16 = mybir.dt.uint16


class Kernel:

    def __init__(self, nc, ctx, io):
        self.nc, self.ctx, self.io = nc, ctx, io
        self.x = self.sb(ctx, "x", [P, B, D])
        self.ident = self.sb(ctx, "ident", [P, P])

    def sb(self, ctx, name, shape, dt=F32):
        return ctx.enter_context(self.nc.sbuf_tensor(name, shape, dt))

    def banks(self, ctx, name, n):
        return ctx.enter_context(self.nc.psum_tensor(name, [P, n, BANK], F32))

    def sem(self, ctx, name):
        return ctx.enter_context(self.nc.semaphore(name))


def over(lo, hi, eng, body, peel=1):
    for i in range(lo, min(lo + peel, hi)):
        body(i)
    if lo + peel < hi:
        with eng.Fori(lo + peel, hi) as i:
            body(i)


def layer0_attention(k: Kernel):
    nc, io, x, ident = k.nc, k.io, k.x, k.ident
    H = 8
    DQ = P // H
    PAIR = 2 * DQ
    with ExitStack() as ctx:
        sb = lambda *a, **kw: k.sb(ctx, *a, **kw)
        sem = lambda n: k.sem(ctx, n)
        ctxn = sb("a_ctx", [P, B, D])
        ctxt = sb("a_ctxT", [P, DC, B, P])
        stats = sb("a_stats", [P, B, 6])
        mv = sb("a_mv", [P, B, 2])
        rstd = sb("a_rstd", [P, B])
        half = sb("a_half", [P, B])
        gamma = sb("a_gamma", [P, 1])
        hmask = sb("a_hmask", [P, 2])
        rmask = sb("a_rmask", [P, 2, B])
        qm = sb("a_qm", [P, 2, D])
        kb = sb("a_kb", [P, D])
        vT = sb("a_vT", [P, DC, H, PAIR])
        nmax = sb("a_nmax", [P, 2, DC])
        sums = sb("a_sums", [P, 2, DC])
        rsum = sb("a_rsum", [P, 2, DC])
        prob = sb("a_prob", [P, 2, DC, D])
        probT = sb("a_probT", [P, 2, DC, D])
        S = k.banks(ctx, "a_S", 2)
        PT = k.banks(ctx, "a_PT", 2)
        R = k.banks(ctx, "a_R", 1)

        x_in = sem("a_x_in")
        small_in = sem("a_small_in")
        zeroed = sem("a_zeroed")
        ident_ok = sem("a_ident_ok")
        dchain = sem("a_dchain")
        var_ok = sem("a_var_ok")
        pchain = sem("a_pchain")
        rstd_ok = sem("a_rstd_ok")
        q_ok = sem("a_q_ok")
        kv_ok = sem("a_kv_ok")
        scores_ok = sem("a_scores_ok")
        max_ok = sem("a_max_ok")
        exp_ok = sem("a_exp_ok")
        prob_ok = sem("a_prob_ok")
        turned = sem("a_turned")
        evac_a = sem("a_evac_a")
        evac_d = sem("a_evac_d")
        pv_ok = sem("a_pv_ok")
        x_ok = sem("a_x_ok")
        block = ctx.enter_context(nc.Block())

        @block.sync
        def _(sp):
            sp.dma_start(hmask[:], io["head_mask"]).then_inc(small_in, 16)
            sp.dma_start(gamma[:], io["gamma"]).then_inc(small_in, 16)
            sp.dma_start(x[:], io["x"]).then_inc(x_in, 16)
            sp.dma_start(ctxn[:], io["ctx"]).then_inc(x_in, 16)
            sp.dma_start(ctxt[:], io["ctxT"]).then_inc(x_in, 16)

        @block.gpsimd
        def _(pool):
            pool.memset(ident[:], 0.0).then_inc(zeroed, 1)
            pool.memset(vT[:], 0.0).then_inc(zeroed, 1)
            pool.memset(half[:], -0.5).then_inc(zeroed, 1)
            pool.wait_ge(zeroed, 3)
            pool.affine_select(out=ident[:], in_=ident[:], compare_op=ALU.not_equal, fill=1.0, base=0,
                               pattern=[[-1, P]], channel_multiplier=1).then_inc(ident_ok, 1)
            pool.wait_ge(var_ok, 1)
            pool.tensor_scalar(rstd[:], mv[:, :, 1], EPS, None, ALU.add).then_inc(pchain, 1)
            pool.wait_ge(pchain, 1)
            pool.tensor_tensor(rstd[:], rstd[:], half[:], ALU.pow).then_inc(rstd_ok, 1)
            pool.wait_ge(x_in, 48)

            def values(b):
                if not (isinstance(b, int) and b == 0):
                    pool.wait_ge(scores_ok, b * H)
                pool.tensor_copy(kb[:], ctxn[:, b, :]).then_inc(kv_ok, 1)
                if not (isinstance(b, int) and b == 0):
                    pool.wait_ge(pv_ok, b * H)
                for r in range(2):
                    src = ctxt[:, :, b, :].rearrange("p c (j r d) -> p c j r d", r=2, d=DQ)[:, :, :, r, :]
                    dst = vT[:].rearrange("p c (j r) d -> p c j r d", r=2)[:, :, :, r, r * DQ:(r + 1) * DQ]
                    for c in range(DC):
                        ins = pool.tensor_copy(dst[:, c], src[:, c])
                ins.then_inc(kv_ok, 1)
            over(0, B, pool, values)

        @block.vector
        def _(dve):
            dve.wait_ge(x_in, 48)
            for b in range(B):
                dve.bn_stats(stats[:, b, :], x[:, b, :]).then_inc(dchain, 1)
            dve.wait_ge(dchain, B)
            for b in range(B):
                ins = dve.bn_aggr(mv[:, b, :], stats[:, b, :])
            ins.then_inc(var_ok, 1)
            dve.wait_ge(rstd_ok, 1)
            dve.wait_ge(small_in, 32)
            for r in range(2):
                dve.tensor_scalar(rmask[:, r, :], rstd[:], hmask[:, r:r + 1], None, ALU.mult).then_inc(dchain, 1)
            dve.wait_ge(dchain, B + 2)

            def head_max(b, h):
                dve.wait_ge(scores_ok, b * H + h + 1)
                dve.tensor_reduce(nmax[:, h % 2, :], S[:, h % 2, :].rearrange("p (c l) -> p c l", c=DC),
                                  AX.X, ALU.min).then_inc(max_ok, 1)

            def scale(b, h):
                dve.wait_ge(exp_ok, b * H + h + 1)
                dve.reciprocal(rsum[:, h % 2, :], sums[:, h % 2, :]).then_inc(dchain, 1)
                dve.wait_ge(dchain, B + 2 + b * H + h + 1)
                for c in range(DC):
                    ins = dve.tensor_scalar(prob[:, h % 2, c, :], prob[:, h % 2, c, :],
                                            rsum[:, h % 2, c:c + 1], None, ALU.mult)
                ins.then_inc(prob_ok, 1)

            def evacuate(b, h):
                dve.wait_ge(turned, b * H + h + 1)
                if not (isinstance(b, int) and b * H + h < 2):
                    dve.wait_ge(pv_ok, b * H + h - 1)
                dve.tensor_copy(probT[:, h % 2].rearrange("p c q -> p (c q)"), PT[:, h % 2, :]).then_inc(evac_d, 1)

            def batch(b):
                if not (isinstance(b, int) and b == 0):
                    dve.wait_ge(scores_ok, b * H)
                for r in range(2):
                    ins = dve.tensor_scalar(qm[:, r, :], x[:, b, :], mv[:, b, 0:1], rmask[:, r, bass.ts(b, 1)],
                                            ALU.subtract, ALU.mult)
                ins.then_inc(q_ok, 1)
                for h in range(H + 2):
                    if h < H:
                        head_max(b, h)
                    if 1 <= h <= H:
                        scale(b, h - 1)
                    if h >= 2 and h % 2 == 1:
                        evacuate(b, h - 2)
                dve.wait_ge(pv_ok, (b + 1) * H)
                dve.scalar_tensor_tensor(out=x[:, b, :], in0=R[:, 0, 0:D], scalar=gamma[:, 0:1],
                                         in1=x[:, b, :], op0=ALU.mult, op1=ALU.add).then_inc(x_ok, 1)
            over(0, B, dve, batch)

        @block.scalar
        def _(act):
            def exps(b, h):
                act.wait_ge(max_ok, b * H + h + 1)
                if not (isinstance(b, int) and b * H + h < 2):
                    act.wait_ge(turned, b * H + h - 1)
                for c in range(DC):
                    ins = act.activation(prob[:, h % 2, c, :], S[:, h % 2, c * D:(c + 1) * D], ACT.Exp,
                                         bias=nmax[:, h % 2, c:c + 1], scale=-1.0,
                                         accum_out=sums[:, h % 2, c:c + 1])
                ins.then_inc(exp_ok, 1)

            def evacuate(b, h):
                act.wait_ge(turned, b * H + h + 1)
                if not (isinstance(b, int) and b * H + h < 2):
                    act.wait_ge(pv_ok, b * H + h - 1)
                act.activation(probT[:, h % 2].rearrange("p c q -> p (c q)"), PT[:, h % 2, :],
                               ACT.Copy).then_inc(evac_a, 1)

            def batch(b):
                for h in range(H + 2):
                    if h < H:
                        exps(b, h)
                    if h >= 2 and h % 2 == 0:
                        evacuate(b, h - 2)
            over(0, B, act, batch)

        @block.tensor
        def _(pe):
            pe.wait_ge(ident_ok, 1)

            def scores(b, h):
                if h == 0:
                    pe.wait_ge(q_ok, b + 1)
                    pe.wait_ge(kv_ok, 2 * b + 1)
                if not (isinstance(b, int) and b * H + h < 2):
                    pe.wait_ge(exp_ok, b * H + h - 1)
                rows = slice(h // 2 * PAIR, (h // 2 + 1) * PAIR)
                for c in range(DC):
                    mm = pe.matmul(S[:, h % 2, c * D:(c + 1) * D], qm[rows, h % 2, c * P:(c + 1) * P],
                                   kb[rows, :], start=True, stop=True)
                mm.then_inc(scores_ok, 1)

            def turn(b, h):
                pe.wait_ge(prob_ok, b * H + h + 1)
                if not (isinstance(b, int) and b * H + h < 2):
                    pe.wait_ge((evac_a, evac_d)[h % 2], b * (H // 2) + h // 2)
                for lc in range(DC):
                    for qc in range(DC):
                        mm = pe.transpose(PT[:, h % 2, lc * D + qc * P:lc * D + (qc + 1) * P],
                                          prob[:, h % 2, qc, lc * P:(lc + 1) * P], ident[:])
                mm.then_inc(turned, 1)

            def weighted(b, h):
                pe.wait_ge((evac_a, evac_d)[h % 2], b * (H // 2) + h // 2 + 1)
                if h == 0:
                    pe.wait_ge(kv_ok, 2 * b + 2)
                    if not (isinstance(b, int) and b == 0):
                        pe.wait_ge(x_ok, b)
                rows = slice(h // 2 * PAIR, (h // 2 + 1) * PAIR)
                for lc in range(DC):
                    mm = pe.matmul(R[rows, 0, 0:D], vT[:, lc, h, :], probT[:, h % 2, lc, :],
                                   start=(h % 2 == 0 and lc == 0), stop=(h % 2 == 1 and lc == DC - 1))
                mm.then_inc(pv_ok, 1)

            def batch(b):
                for h in range(H + 2):
                    if h < H:
                        scores(b, h)
                    if 1 <= h <= H:
                        turn(b, h - 1)
                    if h >= 2:
                        weighted(b, h - 2)
            over(0, B, pe, batch)


class Moe:

    def __init__(self, tag, experts, hidden, topk, clipped):
        self.tag, self.experts, self.hidden, self.topk, self.clipped = tag, experts, hidden, topk, clipped


def moe(k: Kernel, m: Moe, src):
    nc, io, x, ident, tag = k.nc, k.io, k.x, k.ident, m.tag
    E, TOPK, F = m.experts, m.topk, m.hidden
    FC = F // P
    with ExitStack() as outer:
        XT = k.sb(outer, f"{tag}_XT", [P, DC, T])
        route = k.sb(outer, f"{tag}_route", [P, B, E])
        route_tokens(k, m, src, XT, route)
        experts_over_tokens(k, m, XT, route)


def route_tokens(k: Kernel, m: Moe, src, XT, route):
    nc, io, x, ident, tag = k.nc, k.io, k.x, k.ident, m.tag
    E, TOPK = m.experts, m.topk
    PAD = 8
    with ExitStack() as ctx:
        sb = lambda n, s, dt=F32: k.sb(ctx, f"{tag}_{n}", s, dt)
        sem = lambda n: k.sem(ctx, f"{tag}_{n}")
        stats = sb("stats", [P, GRP, 6])
        mv = sb("mv", [P, GRP, 2])
        sq = sb("sq", [P, GRP, D])
        rstd = sb("rstd", [P, GRP])
        half = sb("half", [P, GRP])
        norm = sb("norm", [P, GRP, D])
        grpT = sb("grpT", [P, DC, GRP * P])
        chan = sb("chan", [P, DC, 2])
        rw = sb("rw", [P, DC, E])
        rb = sb("rb", [P, E])
        logit = sb("logit", [P, GRP, E + PAD])
        top = sb("top", [P, GRP, 8])
        taken = sb("taken", [P, GRP, 8])
        marked = sb("marked", [P, GRP, E + PAD])
        ex = sb("ex", [P, GRP, E])
        total = sb("total", [P, GRP])
        TP = k.banks(ctx, f"{tag}_TP", DC)
        LG = k.banks(ctx, f"{tag}_LG", 1)
        loaded = sem("loaded")
        consts = sem("consts")
        chain = sem("chain")
        pchain = sem("pchain")
        var_ok = sem("var_ok")
        rstd_ok = sem("rstd_ok")
        norm_ok = sem("norm_ok")
        turned = sem("turned")
        grp_ok = sem("grp_ok")
        copied = sem("copied")
        logit_ok = sem("logit_ok")
        diff_ok = sem("diff_ok")
        exp_ok = sem("exp_ok")
        rms = m.tag == "e"
        if m.clipped:
            db = sb("db", [E, D])
            wT = sb("wT", [E, GRP * P])
            WT = k.banks(ctx, f"{tag}_WT", 1)
            DB = k.banks(ctx, f"{tag}_DB", GRP * D // BANK)
            route_ok = sem("route_ok")
            wt_turned = sem("wt_turned")
            wt_ok = sem("wt_ok")
            bias_ok = sem("bias_ok")
            bias_used = sem("bias_used")
        block = ctx.enter_context(nc.Block())

        @block.sync
        def _(sp):
            sp.dma_start(rw[:], io[f"{tag}_rw"]).then_inc(loaded, 16)
            sp.dma_start(rb[:], io[f"{tag}_rb"]).then_inc(loaded, 16)
            sp.dma_start(chan[:], io[f"{tag}_chan"]).then_inc(loaded, 16)
            if m.clipped:
                sp.dma_start(db[:], io[f"{tag}_db"]).then_inc(loaded, 16)
        LOADED = 64 if m.clipped else 48

        @block.gpsimd
        def _(pool):
            pool.memset(half[:], -0.5).then_inc(consts, 1)
            pool.memset(logit[:], -BIG).then_inc(consts, 1)
            pool.memset(taken[:], -BIG).then_inc(consts, 1)
            pool.wait_ge(consts, 3)

            def group(g):
                pool.wait_ge(var_ok, g + 1)
                if g:
                    pool.wait_ge(norm_ok, g)
                pool.tensor_scalar(rstd[:], mv[:, :, 1], EPS, None, ALU.add).then_inc(pchain, 1)
                pool.wait_ge(pchain, g + 1)
                pool.tensor_tensor(rstd[:], rstd[:], half[:], ALU.pow).then_inc(rstd_ok, 1)
                pool.wait_ge(grp_ok, g + 1)
                pool.tensor_copy(XT[:, :, g * GRP * P:(g + 1) * GRP * P], grpT[:]).then_inc(copied, 1)
            for g in range(NG):
                group(g)

        @block.scalar
        def _(act):
            act.wait_ge(loaded, LOADED)

            def group(g):
                act.wait_ge(turned, g + 1)
                if g:
                    act.wait_ge(logit_ok, g)
                    act.wait_ge(copied, g)
                for c in range(DC):
                    ins = act.activation(grpT[:, c, :], TP[:, c, :], ACT.Identity, bias=chan[:, c, 1:2],
                                         scale=chan[:, c, 0:1])
                ins.then_inc(grp_ok, 1)
                act.wait_ge(diff_ok, g + 1)
                act.activation(ex[:], ex[:], ACT.Exp).then_inc(exp_ok, 1)
                if m.clipped:
                    act.wait_ge(wt_turned, g + 1)
                    act.activation(wT[:], WT[0:E, 0, :], ACT.Copy).then_inc(wt_ok, 1)
            for g in range(NG):
                group(g)

        @block.tensor
        def _(pe):
            pe.wait_ge(loaded, LOADED)

            def group(g):
                pe.wait_ge(norm_ok, g + 1)
                if g:
                    pe.wait_ge(grp_ok, g)
                for t in range(GRP):
                    for c in range(DC):
                        mm = pe.transpose(TP[:, c, t * P:(t + 1) * P], norm[:, t, c * P:(c + 1) * P], ident[:])
                mm.then_inc(turned, 1)
                pe.wait_ge(grp_ok, g + 1)
                if g:
                    pe.wait_ge(diff_ok, g)
                for t in range(GRP):
                    for c in range(DC):
                        mm = pe.matmul(LG[:, 0, t * E:(t + 1) * E], grpT[:, c, t * P:(t + 1) * P], rw[:, c, :],
                                       start=(c == 0), stop=(c == DC - 1))
                mm.then_inc(logit_ok, 1)
                if m.clipped:
                    pe.wait_ge(route_ok, g + 1)
                    if g:
                        pe.wait_ge(wt_ok, g)
                    for t in range(GRP):
                        mm = pe.transpose(WT[0:E, 0, t * P:(t + 1) * P], ex[:, t, :], ident[:])
                    mm.then_inc(wt_turned, 1)
                    pe.wait_ge(wt_ok, g + 1)
                    if g:
                        pe.wait_ge(bias_used, g)
                    for t in range(GRP):
                        mm = pe.matmul(DB[:, t // 2, t % 2 * D:(t % 2 + 1) * D], wT[:, t * P:(t + 1) * P], db[:],
                                       start=True, stop=True)
                    mm.then_inc(bias_ok, 1)
            for g in range(NG):
                group(g)

        @block.vector
        def _(dve):
            dve.wait_ge(consts, 3)
            dve.wait_ge(loaded, LOADED)
            STEPS = 9 + (TOPK and 0)

            def group(g):
                n = [0]

                def then(ins):
                    n[0] += 1
                    ins.then_inc(chain, 1)
                    dve.wait_ge(chain, g * STEPS + n[0])

                if g:
                    dve.wait_ge(rstd_ok, g)
                if rms:
                    for t in range(GRP):
                        ins = dve.scalar_tensor_tensor(out=sq[:, t, :], in0=src[:, g * GRP + t, :], scalar=1.0,
                                                       in1=src[:, g * GRP + t, :], op0=ALU.mult, op1=ALU.mult,
                                                       accum_out=mv[:, t, 1:2])
                    then(ins)
                    then(dve.tensor_scalar(mv[:, :, 1], mv[:, :, 1], 1.0 / D, None, ALU.mult))
                    then(dve.memset(mv[:, :, 0], 0.0))
                else:
                    for t in range(GRP):
                        ins = dve.bn_stats(stats[:, t, :], src[:, g * GRP + t, :])
                    then(ins)
                    for t in range(GRP):
                        ins = dve.bn_aggr(mv[:, t, :], stats[:, t, :])
                    then(ins)
                    then(dve.tensor_copy(sq[:, 0, 0:1], mv[:, 0, 0:1]))
                dve.sem_inc(var_ok, 1)
                dve.wait_ge(rstd_ok, g + 1)
                if g:
                    dve.wait_ge(turned, g)
                for t in range(GRP):
                    ins = dve.tensor_scalar(norm[:, t, :], src[:, g * GRP + t, :], mv[:, t, 0:1],
                                            rstd[:, t:t + 1], ALU.subtract, ALU.mult)
                ins.then_inc(norm_ok, 1)
                dve.wait_ge(logit_ok, g + 1)
                then(dve.tensor_tensor(logit[:, :, 0:E], LG[:, 0, 0:GRP * E].rearrange("p (t e) -> p t e", t=GRP),
                                       rb[:, None, :].to_broadcast([P, GRP, E]), ALU.add))
                for t in range(GRP):
                    ins = dve.max(top[:, t, :], logit[:, t, :])
                then(ins)
                if m.clipped and g:
                    dve.wait_ge(wt_turned, g)
                dve.tensor_tensor(ex[:], logit[:, :, 0:E], top[:, :, 0:1].to_broadcast([P, GRP, E]),
                                  ALU.subtract).then_inc(diff_ok, 1)
                then(dve.tensor_copy(taken[:, :, 0:TOPK], top[:, :, 0:TOPK]))
                for t in range(GRP):
                    ins = dve.match_replace(out=marked[:, t, :], in_to_replace=taken[:, t, :],
                                            in_values=logit[:, t, :], imm_value=BIG)
                then(ins)
                then(dve.tensor_scalar(marked[:, :, 0:E], marked[:, :, 0:E], BIG, None, ALU.is_ge))
                dve.wait_ge(exp_ok, g + 1)
                then(dve.tensor_tensor(ex[:], ex[:], marked[:, :, 0:E], ALU.mult))
                dve.tensor_reduce(total[:], ex[:], AX.X, ALU.add).then_inc(chain2, 1)
                dve.wait_ge(chain2, 3 * g + 1)
                dve.reciprocal(total[:], total[:]).then_inc(chain2, 1)
                dve.wait_ge(chain2, 3 * g + 2)
                dve.tensor_tensor(ex[:], ex[:], total[:, :, None].to_broadcast([P, GRP, E]),
                                  ALU.mult).then_inc(chain2, 1)
                dve.wait_ge(chain2, 3 * g + 3)
                last = dve.tensor_copy(route[:, g * GRP:(g + 1) * GRP, :], ex[:])
                if m.clipped:
                    last.then_inc(route_ok, 1)
                    dve.wait_ge(bias_ok, g + 1)
                    for t in range(0, GRP, 2):
                        ins = dve.tensor_tensor(x[:, g * GRP + t:g * GRP + t + 2, :],
                                                DB[:, t // 2, :].rearrange("p (t d) -> p t d", t=2),
                                                x[:, g * GRP + t:g * GRP + t + 2, :], ALU.add)
                    ins.then_inc(bias_used, 1)
            chain2 = sem("chain2")
            for g in range(NG):
                group(g)


def experts_over_tokens(k: Kernel, m: Moe, XT, route):
    nc, io, x, tag = k.nc, k.io, k.x, m.tag
    E, F = m.experts, m.hidden
    FC = F // P
    SLOTS = 2
    UNITS = NG * FC
    with ExitStack() as ctx:
        sb = lambda n, s, dt=F32: k.sb(ctx, f"{tag}x_{n}", s, dt)
        sem = lambda n: k.sem(ctx, f"{tag}x_{n}")
        w_in = sb("w_in", [P, SLOTS, 2, DC, F])
        w_out = sb("w_out", [P, SLOTS, FC, D])
        bias = sb("bias", [P, SLOTS, 2, FC])
        HB = 2 * FC
        gate = sb("gate", [P, 2, BANK])
        up = sb("up", [P, 2, BANK])
        sig = sb("sig", [P, 2, BANK])
        hT = sb("hT", [P, 2, FC, BANK])
        GU = k.banks(ctx, f"{tag}x_GU", 4)
        OUT = k.banks(ctx, f"{tag}x_OUT", 4)
        w_ok = [sem(f"w_ok{s}") for s in range(SLOTS)]
        gate_up = sem("gate_up")
        gu_free = sem("gu_free")
        gate_ok = sem("gate_ok")
        sig_ok = sem("sig_ok")
        glu_ok = sem("glu_ok")
        up_ok = sem("up_ok")
        h_ok = sem("h_ok")
        out_ok = sem("out_ok")
        out_used = sem("out_used")
        block = ctx.enter_context(nc.Block())
        LOADS = 3 if m.clipped else 2

        def started(n, s, j):
            return not isinstance(n, int) or n + s > 0 or j >= 0

        def unit(n, s, g, f):
            return (SLOTS * n + s) * UNITS + g * FC + f

        def both(eng, body):
            def pair(n):
                for s in range(SLOTS):
                    body(n, s)
            pair(0)
            with eng.Fori(1, E // SLOTS) as n:
                pair(n)

        @block.sync
        def _(sp):
            def load(n, s):
                if not isinstance(n, int):
                    sp.wait_ge(out_ok, (SLOTS * n + s - SLOTS + 1) * NG)
                sp.dma_start(w_in[:, s], io[f"{tag}_w_in"][SLOTS * n + s]).then_inc(w_ok[s], 16)
                sp.dma_start(w_out[:, s], io[f"{tag}_w_out"][SLOTS * n + s]).then_inc(w_ok[s], 16)
                if m.clipped:
                    sp.dma_start(bias[:, s], io[f"{tag}_bias"][SLOTS * n + s]).then_inc(w_ok[s], 16)
            both(sp, load)

        def loaded(eng, n, s):
            eng.wait_ge(w_ok[s], (n + 1) * (16 * LOADS))

        @block.tensor
        def _(pe):
            def project(n, s, g, f):
                u = unit(n, s, g, f)
                if g == 0 and f == 0:
                    loaded(pe, n, s)
                if started(n, s, g * FC + f - 2):
                    pe.wait_ge(gu_free if m.clipped else h_ok, u - 1)
                for half in range(2):
                    for c in range(DC):
                        mm = pe.matmul(GU[:, 2 * (f % 2) + half, :], w_in[:, s, half, c, f * P:(f + 1) * P],
                                       XT[:, c, g * BANK:(g + 1) * BANK], start=(c == 0), stop=(c == DC - 1))
                mm.then_inc(gate_up, 1)

            def down(n, s, g):
                turn = (SLOTS * n + s) * NG + g
                pe.wait_ge(h_ok, (SLOTS * n + s) * UNITS + (g + 1) * FC)
                if started(n, s, g - 2):
                    pe.wait_ge(out_used, turn - 1)
                for t in range(GRP):
                    for f in range(FC):
                        mm = pe.matmul(OUT[:, 2 * (g % 2) + t // 2, t % 2 * D:(t % 2 + 1) * D],
                                       hT[:, g % 2, f, t * P:(t + 1) * P], w_out[:, s, f, :],
                                       start=(f == 0), stop=(f == FC - 1))
                mm.then_inc(out_ok, 1)

            def expert(n, s):
                for g in range(NG):
                    for f in range(FC):
                        project(n, s, g, f)
                        if f == FC // 2 - 1 and g > 0:
                            down(n, s, g - 1)
                down(n, s, NG - 1)
            both(pe, expert)

        @block.scalar
        def _(act):
            def expert(n, s):
                for g in range(NG):
                    for f in range(FC):
                        u = unit(n, s, g, f)
                        if m.clipped:
                            act.wait_ge(gate_ok, u + 1)
                            if started(n, s, g * FC + f - 2):
                                act.wait_ge(glu_ok, u - 1)
                            act.activation(sig[:, f % 2, :], gate[:, f % 2, :], ACT.Sigmoid,
                                           scale=1.702).then_inc(sig_ok, 1)
                        else:
                            act.wait_ge(gate_up, u + 1)
                            if started(n, s, g * FC + f - 2):
                                act.wait_ge(h_ok, u - 1)
                            act.activation(sig[:, f % 2, :], GU[:, 2 * (f % 2), :], ACT.Silu).then_inc(sig_ok, 1)
            both(act, expert)

        if m.clipped:
            @block.gpsimd
            def _(pool):
                def expert(n, s):
                    for g in range(NG):
                        for f in range(FC):
                            u = unit(n, s, g, f)
                            pool.wait_ge(sig_ok, u + 1)
                            pool.tensor_tensor(sig[:, f % 2, :], gate[:, f % 2, :], sig[:, f % 2, :],
                                               ALU.mult).then_inc(glu_ok, 1)
                both(pool, expert)

        @block.vector
        def _(dve):
            def clip(n, s, g, f):
                u = unit(n, s, g, f)
                if g == 0 and f == 0:
                    loaded(dve, n, s)
                dve.wait_ge(gate_up, u + 1)
                if started(n, s, g * FC + f - 2):
                    dve.wait_ge(glu_ok, u - 1)
                dve.tensor_scalar(gate[:, f % 2, :], GU[:, 2 * (f % 2), :], bias[:, s, 0, f:f + 1], 7.0,
                                  ALU.add, ALU.min).then_inc(gate_ok, 1)
                dve.tensor_scalar(up[:, f % 2, :], GU[:, 2 * (f % 2) + 1, :], bias[:, s, 1, f:f + 1], 7.0,
                                  ALU.add, ALU.min).then_inc(gu_free, 1)

            def gated(n, s, g, f):
                u = unit(n, s, g, f)
                dve.wait_ge(gu_free, u + 1)
                dve.tensor_scalar(up[:, f % 2, :], up[:, f % 2, :], -7.0, 1.0, ALU.max, ALU.add).then_inc(up_ok, 1)
                dve.wait_ge(up_ok, u + 1)
                dve.wait_ge(glu_ok, u + 1)
                if f == 0 and started(n, s, g - 2):
                    dve.wait_ge(out_ok, (SLOTS * n + s) * NG + g - 1)
                dve.tensor_tensor(hT[:, g % 2, f, :], up[:, f % 2, :], sig[:, f % 2, :], ALU.mult)\
                   .then_inc(h_ok, 1)

            def swiglu(n, s, g, f):
                u = unit(n, s, g, f)
                if g == 0 and f == 0:
                    loaded(dve, n, s)
                dve.wait_ge(sig_ok, u + 1)
                if f == 0 and started(n, s, g - 2):
                    dve.wait_ge(out_ok, (SLOTS * n + s) * NG + g - 1)
                dve.tensor_tensor(hT[:, g % 2, f, :], GU[:, 2 * (f % 2) + 1, :], sig[:, f % 2, :], ALU.mult)\
                   .then_inc(h_ok, 1)

            def add(n, s, g):
                dve.wait_ge(out_ok, (SLOTS * n + s) * NG + g + 1)
                for t in range(GRP):
                    ins = dve.scalar_tensor_tensor(
                        out=x[:, g * GRP + t, :], in0=OUT[:, 2 * (g % 2) + t // 2, t % 2 * D:(t % 2 + 1) * D],
                        scalar=route[:, g * GRP + t, bass.ds(SLOTS * n + s, 1)], in1=x[:, g * GRP + t, :],
                        op0=ALU.mult, op1=ALU.add)
                ins.then_inc(out_used, 1)

            def expert(n, s):
                for g in range(NG):
                    for f in range(FC):
                        if m.clipped:
                            clip(n, s, g, f)
                            if f > 0:
                                gated(n, s, g, f - 1)
                        else:
                            swiglu(n, s, g, f)
                    if m.clipped:
                        gated(n, s, g, FC - 1)
                    if g > 0:
                        add(n, s, g - 1)
                add(n, s, NG - 1)
            both(dve, expert)


def double_norm(k: Kernel, tag, rms, finish):
    nc, io, x, ident = k.nc, k.io, k.x, k.ident
    with ExitStack() as ctx:
        sb = lambda n, s, dt=F32: k.sb(ctx, f"{tag}n_{n}", s, dt)
        sem = lambda n: k.sem(ctx, f"{tag}n_{n}")
        stats = sb("stats", [P, 2, GRP, 6])
        mv = sb("mv", [P, 2, GRP, 2])
        sq = sb("sq", [P, GRP, D])
        rstd = sb("rstd", [P, 2, GRP])
        half = sb("half", [P, GRP])
        first = sb("first", [P, GRP, D])
        second = sb("second", [P, GRP, D])
        finT = sb("finT", [P, DC, GRP * P])
        chan = sb("chan", [P, DC, 2])
        TP = k.banks(ctx, f"{tag}n_TP", DC)
        loaded = sem("loaded")
        consts = sem("consts")
        chain = sem("chain")
        pchain = sem("pchain")
        var_ok = sem("var_ok")
        rstd_ok = sem("rstd_ok")
        norm_ok = sem("norm_ok")
        turned = sem("turned")
        fin_ok = sem("fin_ok")
        fin_used = sem("fin_used")
        finish.open(k, ctx)
        block = ctx.enter_context(nc.Block())

        @block.sync
        def _(sp):
            sp.dma_start(chan[:], io[f"{tag}_chan"]).then_inc(loaded, 16)
            finish.sync(sp)

        @block.gpsimd
        def _(pool):
            pool.memset(half[:], -0.5).then_inc(consts, 1)
            pool.memset(mv[:], 0.0).then_inc(consts, 1)
            pool.wait_ge(consts, 2)
            for g in range(NG):
                for j in range(2):
                    n = 2 * g + j
                    pool.wait_ge(var_ok, n + 1)
                    pool.tensor_scalar(rstd[:, j, :], mv[:, j, :, 1], EPS, None, ALU.add).then_inc(pchain, 1)
                    pool.wait_ge(pchain, n + 1)
                    pool.tensor_tensor(rstd[:, j, :], rstd[:, j, :], half[:], ALU.pow).then_inc(rstd_ok, 1)

        @block.tensor
        def _(pe):
            for g in range(NG):
                pe.wait_ge(norm_ok, g + 1)
                if g:
                    pe.wait_ge(fin_ok, g)
                for t in range(GRP):
                    for c in range(DC):
                        mm = pe.transpose(TP[:, c, t * P:(t + 1) * P], second[:, t, c * P:(c + 1) * P], ident[:])
                mm.then_inc(turned, 1)

        @block.scalar
        def _(act):
            act.wait_ge(loaded, 16)
            for g in range(NG):
                act.wait_ge(turned, g + 1)
                if g:
                    act.wait_ge(fin_used, g)
                for c in range(DC):
                    ins = act.activation(finT[:, c, :], TP[:, c, :], ACT.Identity, bias=chan[:, c, 1:2],
                                         scale=chan[:, c, 0:1])
                ins.then_inc(fin_ok, 1)

        @block.vector
        def _(dve):
            count = [0]

            def then(ins):
                count[0] += 1
                ins.then_inc(chain, 1)
                dve.wait_ge(chain, count[0])

            def statistics(j, src):
                for t in range(GRP):
                    ins = dve.bn_stats(stats[:, j, t, :], src(t))
                then(ins)
                for t in range(GRP):
                    ins = dve.bn_aggr(mv[:, j, t, :], stats[:, j, t, :])
                ins.then_inc(var_ok, 1)

            def mean_square(src):
                for t in range(GRP):
                    ins = dve.scalar_tensor_tensor(out=sq[:, t, :], in0=src(t), scalar=1.0 / D, in1=src(t),
                                                   op0=ALU.mult, op1=ALU.mult, accum_out=mv[:, 1, t, 1:2])
                ins.then_inc(var_ok, 1)

            dve.wait_ge(consts, 2)
            finish.start(dve, then)
            for g in range(NG):
                statistics(0, lambda t: x[:, g * GRP + t, :])
                dve.wait_ge(rstd_ok, 2 * g + 1)
                for t in range(GRP):
                    ins = dve.tensor_scalar(first[:, t, :], x[:, g * GRP + t, :], mv[:, 0, t, 0:1],
                                            rstd[:, 0, t:t + 1], ALU.subtract, ALU.mult)
                then(ins)
                finish.normed(dve, g, first)
                if rms:
                    mean_square(lambda t: first[:, t, :])
                else:
                    statistics(1, lambda t: first[:, t, :])
                dve.wait_ge(rstd_ok, 2 * g + 2)
                if g:
                    dve.wait_ge(turned, g)
                for t in range(GRP):
                    ins = dve.tensor_scalar(second[:, t, :], first[:, t, :], mv[:, 1, t, 0:1],
                                            rstd[:, 1, t:t + 1], ALU.subtract, ALU.mult)
                ins.then_inc(norm_ok, 1)
                dve.wait_ge(fin_ok, g + 1)
                finish.group(dve, g, finT, then).then_inc(fin_used, 1)


FP8_MAX = 448.0
FP8_NORMAL = 2.0 ** -6
FP8_SHIFT = 2.0 ** 7


def round_fp8(dve, y, big, out, then, last=None):
    then(dve.tensor_scalar(y, y, -FP8_MAX, None, ALU.max))
    then(dve.tensor_scalar(big.bitcast(U16), y.bitcast(U16), 0x7FFF, None, ALU.bitwise_and))
    then(dve.tensor_scalar(big, big.bitcast(BF16), 1.5 * FP8_NORMAL, FP8_SHIFT, ALU.max, ALU.mult))
    then(dve.tensor_tensor(y.bitcast(F16), y, big, ALU.add))
    return dve.tensor_tensor(out, y.bitcast(F16), big, ALU.subtract)


class Quantise:

    def __init__(self, xq, w, wp, scales):
        self.xq, self.w, self.wp, self.scales = xq, w, wp, scales

    def open(self, k, ctx):
        self.k = k
        self.raw = k.sb(ctx, "c_raw", [P, 8, 4, D])
        self.y = k.sb(ctx, "c_y", [P, DC, GRP * P], BF16)
        self.big = k.sb(ctx, "c_big", [P, DC, GRP * P], F16)
        self.ws = k.sb(ctx, "c_ws", [P, 4, DC])
        self.inv = k.sb(ctx, "c_inv", [P, 4, DC])
        self.mean = k.sb(ctx, "c_mean", [P, 8 * DC, 6])
        self.in_scale = k.sb(ctx, "c_in_scale", [P, 4, DC])
        self.w_scale = k.sb(ctx, "c_w_scale", [P, 4])
        self.p_scale = k.sb(ctx, "c_p_scale", [P, 2])
        self.smooth = k.sb(ctx, "c_smooth", [P, 8, 4])
        self.ok = k.sem(ctx, "c_loaded")

    def sync(self, sp):
        io = self.k.io
        for t, n in ((self.w, "c_w"), (self.raw, "c_wp"), (self.in_scale, "c_in_scale"),
                     (self.w_scale, "c_w_scale"), (self.p_scale, "c_p_scale"), (self.smooth, "c_smooth")):
            sp.dma_start(t[:], io[n]).then_inc(self.ok, 16)

    def start(self, dve, then):
        sc = self.scales
        dve.wait_ge(self.ok, 96)
        then(dve.reciprocal(self.inv[:], self.in_scale[:]))
        then(dve.reciprocal(sc["smooth"][:], self.smooth[:]))
        then(dve.tensor_tensor(sc["proj"][:], self.p_scale[:, 0:1], self.p_scale[:, 1:2], ALU.mult))
        then(dve.tensor_tensor(self.ws[:], self.in_scale[:], self.w_scale[:, :, None].to_broadcast([P, 4, DC]),
                               ALU.mult))
        for v, (a, b) in enumerate(((0, 2), (2, 4), (4, 5), (6, 7))):
            for c in range(DC):
                part = self.w[:, :, c, a * P:b * P]
                ins = dve.tensor_scalar(part, part, self.ws[:, v, c:c + 1], None, ALU.mult)
        then(ins)
        heads = self.w[:].rearrange("p g c (s d) -> p (g c) s d", d=P)[:, :, 0:6, :]
        then(dve.tensor_reduce(self.mean[:], heads, AX.X, ALU.add))
        then(dve.tensor_scalar(self.mean[:], self.mean[:], 1.0 / P, None, ALU.mult))
        for s in range(6):
            ins = dve.tensor_tensor(heads[:, :, s, :], heads[:, :, s, :],
                                    self.mean[:, :, s:s + 1].to_broadcast([P, 8 * DC, P]), ALU.subtract)
        then(ins)
        then(dve.tensor_copy(self.wp[:, 0], self.raw[:]))
        then(dve.tensor_tensor(self.wp[:, 1], self.raw[:], self.wp[:, 0], ALU.subtract))

    def normed(self, dve, g, first):
        pass

    def group(self, dve, g, finT, then):
        for v in range(4):
            for c in range(DC):
                ins = dve.tensor_scalar(self.y[:, c, :], finT[:, c, :], self.inv[:, v, c:c + 1], FP8_MAX,
                                        ALU.mult, ALU.min)
            then(ins)
            ins = round_fp8(dve, self.y[:], self.big[:], self.xq[:, v, :, g * GRP * P:(g + 1) * GRP * P], then)
            if v < 3:
                then(ins)
        return ins


class Keep:

    def __init__(self, nT, h):
        self.nT, self.h = nT, h

    def open(self, k, ctx):
        pass

    def sync(self, sp):
        pass

    def start(self, dve, then):
        pass

    def normed(self, dve, g, first):
        dve.tensor_copy(self.h[:, g * GRP:(g + 1) * GRP, :], first[:])

    def group(self, dve, g, finT, then):
        return dve.tensor_copy(self.nT[:, :, g * GRP * P:(g + 1) * GRP * P], finT[:])


def ticks(eng, steps, stages):
    lo, hi = min(l for l, _ in stages), 3
    first = 6

    def tick(t, s, inside):
        for lag, f in stages:
            if inside or 0 <= t - lag < steps:
                f(t - lag, (s - lag) % 2)
    for t in range(-1, first):
        tick(t, t, False)
    n_in = (steps - 2 - first) // 2
    with eng.Fori(0, n_in) as n:
        for s in range(2):
            for lag, f in stages:
                f(n * 2 + (first + s - lag), (s - lag) % 2)
    for t in range(first + 2 * n_in, steps + 4):
        tick(t, t, False)


def past(u, n):
    return not isinstance(u, int) or u >= n


class CrossForm:
    tag, heads, vheads, turned, groups = "c", 6, 2, 6, 8


class CausalForm:
    tag, heads, vheads, turned, groups = "d", 5, 1, 5, 4


def attention(k: Kernel, form, t):
    nc, io, x, ident, tag = k.nc, k.io, k.x, k.ident, form.tag
    cross = form is CrossForm
    NH = form.heads
    NV = form.vheads
    STEPS = form.groups * B
    KHEAD = [4, 4, 5, 5] if cross else [4, 4, 4, 4]
    XS = 5 if cross else 1
    with ExitStack() as ctx:
        sb = lambda n, s, dt=F32: k.sb(ctx, f"{tag}a_{n}", s, dt)
        sem = lambda n: k.sem(ctx, f"{tag}a_{n}")
        xs = sb("xs", [P, 2, XS, DC, P])
        vnew = sb("vnew", [P, 2, NV, P])
        v = sb("v", [P, 2, NV, P])
        nq = sb("nq", [P, 2, NH, P])
        qk = sb("qk", [P, 2, NH, P])
        nmax = sb("nmax", [P, 2, 4])
        sums = sb("sums", [P, 2, 4])
        rsum = sb("rsum", [P, 2, 4])
        prob = sb("prob", [P, 2, 4, P])
        probT = sb("probT", [P, 2, 4, P])
        cat = sb("cat", [P, 2, 4, P], BF16 if cross else F32)
        QKV = k.banks(ctx, f"{tag}a_QKV", 2)
        TQ = k.banks(ctx, f"{tag}a_TQ", 2)
        S = k.banks(ctx, f"{tag}a_S", 1)
        PT = k.banks(ctx, f"{tag}a_PT", 1)
        O = k.banks(ctx, f"{tag}a_O", 1)
        F = k.banks(ctx, f"{tag}a_F", 1)
        q4 = QKV[:, 0, :].rearrange("p (h d) -> p h d", d=P)
        rest = QKV[:, 1, :].rearrange("p (h d) -> p h d", d=P)
        if cross:
            sq = sb("sq", [P, NH, P])
            ss = sb("ss", [P, 2, NH])
            rstd = sb("rstd", [P, 2, NH])
            half = sb("half", [P, NH])
            y = sb("y", [P, 4, P], BF16)
            big = sb("big", [P, 4, P], F16)
            hw = sb("hw", [P, 4, 2])
        else:
            ra = sb("ra", [P, 2, NH, P])
            rb = sb("rb", [P, 2, NH, P])
            cos = sb("cos", [P, P])
            sin = sb("sin", [P, P])
            identb = sb("identb", [P, P], BF16)
            mask = sb("mask", [P, P], BF16)
        loaded = sem("loaded")
        consts = sem("consts")
        names = ("xs_ok", "proj_ok", "v_ok", "sq_ok", "ss_ok", "rstd_ok", "nq_ok", "rot_ok", "tq_ok", "qk_ok", "s_ok",
                 "min_ok", "exp_ok", "p_ok", "turn_ok", "probT_ok", "o_ok", "cat_ok", "f_ok", "acc_ok",
                 "chain", "qchain", "pchain", "hw_ok", "v_held")
        (xs_ok, proj_ok, v_ok, sq_ok, ss_ok, rstd_ok, nq_ok, rot_ok, tq_ok, qk_ok, s_ok, min_ok, exp_ok, p_ok, turn_ok,
         probT_ok, o_ok, cat_ok, f_ok, acc_ok, chain, qchain, pchain, hw_ok, v_held) = (sem(n) for n in names)
        block = ctx.enter_context(nc.Block())
        batch = lambda u: u % B if isinstance(u, int) else u & (B - 1)
        group = lambda u: u // B if isinstance(u, int) else (u >> 4) & (form.groups - 1)

        @block.sync
        def _(sp):
            if cross:
                sp.dma_start(t["ctxT"][:], io["ctxT"]).then_inc(loaded, 16)
                sp.dma_start(hw[:], io["c_hw"]).then_inc(loaded, 16)
            else:
                sp.dma_start(cos[:], io["d_cos"]).then_inc(loaded, 16)
                sp.dma_start(sin[:], io["d_sin"]).then_inc(loaded, 16)
                sp.dma_start(t["w"][:], io["d_w"]).then_inc(loaded, 16)
                sp.dma_start(t["wo"][:], io["d_wo"]).then_inc(loaded, 16)
        LOADED = 32 if cross else 64

        @block.gpsimd
        def _(pool):
            if cross:
                pool.memset(half[:], -0.5).then_inc(consts, 1)
            else:
                pool.tensor_copy(identb[:], ident[:]).then_inc(consts, 1)
                pool.memset(mask[:], 0.0).then_inc(consts, 1)
                pool.wait_ge(consts, 2)
                pool.affine_select(out=mask[:], in_=mask[:], compare_op=ALU.is_ge, fill=BIG, base=0,
                                   pattern=[[-1, P]], channel_multiplier=1).then_inc(consts, 1)
            pool.wait_ge(consts, 1 if cross else 3)
            pool.wait_ge(loaded, LOADED)

            def tokens(u, p):
                if past(u, 2):
                    pool.wait_ge(proj_ok, u - 1)
                tile = batch(u)
                if cross:
                    pool.tensor_copy(xs[:, p, 4], t["ctxT"][:, :, tile, :])
                    src = t["xq"][:].rearrange("p v c (b s) -> p (v c) b s", s=P)[:, :, tile, :]
                    pool.tensor_copy(xs[:, p, 0:4].rearrange("p v c s -> p (v c) s"), src).then_inc(xs_ok, 1)
                else:
                    src = t["nT"][:].rearrange("p c (b s) -> p c b s", s=P)[:, :, tile, :]
                    pool.tensor_copy(xs[:, p, 0], src).then_inc(xs_ok, 1)

            def spread(u, p):
                pool.wait_ge(ss_ok, u + 1)
                if past(u, 2):
                    pool.wait_ge(nq_ok, u - 1)
                pool.tensor_tensor(rstd[:, p, :], ss[:, p, :], half[:], ALU.pow).then_inc(rstd_ok, 1)

            def rotate(u, p):
                pool.wait_ge(rot_ok, u + 1)
                if past(u, 2):
                    pool.wait_ge(tq_ok, u - 1)
                pool.tensor_tensor(nq[:, p], ra[:, p], rb[:, p], ALU.add).then_inc(nq_ok, 1)

            def may_hold(u, p):
                pool.wait_ge(v_ok, u + 1)
                if past(u, 2):
                    pool.wait_ge(o_ok, u - 1)

            def hold(u, p):
                pool.tensor_copy(v[:, p], vnew[:, p]).then_inc(v_held, 1)
            ticks(pool, STEPS, [(0, spread if cross else rotate), (1, may_hold), (-1, tokens), (1, hold)])

        @block.tensor
        def _(pe):
            pe.wait_ge(loaded, LOADED)
            pe.wait_ge(consts, 1 if cross else 3)
            if cross:
                PARTS = [(0, 0, 2, 0), (0, 2, 4, 1), (1, 0, 1, 2), (1, 2, 3, 3), (1, 1, 2, 4), (1, 3, 4, 4)]
            else:
                PARTS = [(0, 0, 4, 0), (1, 0, 2, 0)]

            def project(u, p):
                pe.wait_ge(xs_ok, u + 1)
                if past(u, 1):
                    pe.wait_ge(nq_ok if cross else rot_ok, u)
                    pe.wait_ge(v_ok, u)
                for bank, a, b, tile in PARTS:
                    for c in range(DC):
                        w = t["w"][:].rearrange("p g c n -> p (g c n)")
                        n = 1024 if cross else 768
                        mm = pe.matmul(QKV[:, bank, a * P:b * P], xs[:, p, tile, c, :],
                                       w[:, bass.ds(group(u) * (DC * n) + c * n + bank * BANK + a * P, (b - a) * P)],
                                       start=(c == 0), stop=(c == DC - 1))
                mm.then_inc(proj_ok, 1)

            def turn_qk(u, p):
                pe.wait_ge(nq_ok, u + 1)
                if past(u, 1):
                    pe.wait_ge(qk_ok, u)
                for h in range(NH):
                    mm = pe.transpose(TQ[:, h // 4, h % 4 * P:(h % 4 + 1) * P], nq[:, p, h, :], ident[:])
                mm.then_inc(tq_ok, 1)

            def scores(u, p):
                pe.wait_ge(qk_ok, u + 1)
                if past(u, 1):
                    pe.wait_ge(exp_ok, u)
                for h in range(4):
                    mm = pe.matmul(S[:, 0, h * P:(h + 1) * P], qk[:, p, h, :], qk[:, p, KHEAD[h], :],
                                   start=True, stop=cross)
                    if not cross:
                        mm = pe.matmul(S[:, 0, h * P:(h + 1) * P], identb[:], mask[:], start=False, stop=True)
                mm.then_inc(s_ok, 1)

            def turn_prob(u, p):
                pe.wait_ge(p_ok, u + 1)
                if past(u, 1):
                    pe.wait_ge(probT_ok, u)
                for h in range(4):
                    mm = pe.transpose(PT[:, 0, h * P:(h + 1) * P], prob[:, p, h, :], ident[:])
                mm.then_inc(turn_ok, 1)

            def weighted(u, p):
                pe.wait_ge(probT_ok, u + 1)
                pe.wait_ge(v_held, u + 1)
                if past(u, 1):
                    pe.wait_ge(cat_ok, u)
                n = 4 // NV
                for j in range(NV):
                    mm = pe.matmul(O[:, 0, j * n * P:(j + 1) * n * P], v[:, p, j, :],
                                   probT[:, p, j * n:(j + 1) * n, :].rearrange("p h q -> p (h q)"),
                                   start=True, stop=True)
                mm.then_inc(o_ok, 1)

            def out_proj(u, p):
                pe.wait_ge(cat_ok, u + 1)
                if past(u, 1):
                    pe.wait_ge(acc_ok, u)
                g = group(u)
                for j in range(4):
                    if cross:
                        wp = t["wp"][:].rearrange("p a g j n -> p a (g j n)")
                        for a in range(2):
                            mm = pe.matmul(F[:, 0, 0:D], cat[:, p, j, :], wp[:, a, bass.ds(g * (4 * D) + j * D, D)],
                                           start=(j == 0 and a == 0), stop=(j == 3 and a == 1))
                    else:
                        wo = t["wo"][:].rearrange("p g j n -> p (g j n)")
                        mm = pe.matmul(F[:, 0, 0:D], cat[:, p, j, :], wo[:, bass.ds(g * (4 * D) + j * D, D)],
                                       start=(j == 0), stop=(j == 3))
                mm.then_inc(f_ok, 1)
            ticks(pe, STEPS, [(0, project), (1, scores), (2, turn_prob), (3, out_proj), (2, weighted), (0, turn_qk)])

        @block.scalar
        def _(act):
            act.wait_ge(loaded, LOADED)
            if cross:
                act.wait_ge(hw_ok, 1)

            def values(u, p):
                act.wait_ge(proj_ok, u + 1)
                if cross:
                    if past(u, 1):
                        act.wait_ge(ss_ok, u)
                    act.activation(sq[:, 0:4, :], q4, ACT.Square)
                    act.activation(sq[:, 4:6, :], rest[:, 0:2, :], ACT.Square)
                if past(u, 2):
                    act.wait_ge(v_held, u - 1)
                a = 2 if cross else 1
                act.activation(vnew[:, p], rest[:, a:a + NV, :], ACT.Copy).then_inc(v_ok, 1)

            def exps(u, p):
                act.wait_ge(min_ok, u + 1)
                if past(u, 2):
                    act.wait_ge(turn_ok, u - 1)
                for h in range(4):
                    ins = act.activation(prob[:, p, h, :], S[:, 0, h * P:(h + 1) * P], ACT.Exp,
                                         bias=nmax[:, p, h:h + 1], scale=-1.0, accum_out=sums[:, p, h:h + 1])
                ins.then_inc(exp_ok, 1)

            def evac_qk(u, p):
                act.wait_ge(tq_ok, u + 1)
                if past(u, 2):
                    act.wait_ge(s_ok, u - 1)
                if cross:
                    for n, (a, b) in enumerate(((0, 2), (2, 4), (4, 5), (5, 6))):
                        ins = act.activation(qk[:, p, a:b, :].rearrange("p h d -> p (h d)"),
                                             TQ[:, a // 4, a % 4 * P:(a % 4 + b - a) * P], ACT.Identity,
                                             bias=hw[:, n, 1:2], scale=hw[:, n, 0:1])
                else:
                    act.activation(qk[:, p, 0:4, :].rearrange("p h d -> p (h d)"), TQ[:, 0, :], ACT.Copy,
                                   scale=-float(P) ** -0.5)
                    ins = act.activation(qk[:, p, 4, :], TQ[:, 1, 0:P], ACT.Copy)
                ins.then_inc(qk_ok, 1)

            ticks(act, STEPS, [(0, values), (1, exps), (0, evac_qk)])

        @block.vector
        def _(dve):
            dve.wait_ge(loaded, LOADED)

            if cross:
                dve.tensor_scalar(hw[:, 0:2, :], hw[:, 0:2, :], -float(P) ** -0.5, None, ALU.mult).then_inc(hw_ok, 1)

            def variance(u, p):
                dve.wait_ge(v_ok, u + 1)
                if past(u, 2):
                    dve.wait_ge(rstd_ok, u - 1)
                dve.tensor_reduce(ss[:, p, :], sq[:], AX.X, ALU.add).then_inc(chain, 1)
                dve.wait_ge(chain, u + 1)
                dve.tensor_scalar(ss[:, p, :], ss[:, p, :], 1.0 / P, EPS, ALU.mult, ALU.add).then_inc(ss_ok, 1)

            def normed(u, p):
                dve.wait_ge(rstd_ok, u + 1)
                if past(u, 2):
                    dve.wait_ge(tq_ok, u - 1)
                dve.tensor_tensor(nq[:, p, 0:4, :], q4, rstd[:, p, 0:4, None].to_broadcast([P, 4, P]), ALU.mult)
                dve.tensor_tensor(nq[:, p, 4:6, :], rest[:, 0:2, :], rstd[:, p, 4:6, None].to_broadcast([P, 2, P]),
                                  ALU.mult).then_inc(nq_ok, 1)

            def rotary(u, p):
                dve.wait_ge(v_ok, u + 1)
                if past(u, 2):
                    dve.wait_ge(nq_ok, u - 1)
                HALF = P // 2
                for src, a, n in ((q4, 0, 4), (rest, 4, 1)):
                    dve.tensor_tensor(ra[:, p, a:a + n, :], src[:, 0:n, :],
                                      cos[:, None, :].to_broadcast([P, n, P]), ALU.mult)
                    for s in range(2):
                        here, there = slice(s * HALF, (s + 1) * HALF), slice((1 - s) * HALF, (2 - s) * HALF)
                        ins = dve.tensor_tensor(rb[:, p, a:a + n, here], src[:, 0:n, there],
                                                sin[:, None, here].to_broadcast([P, n, HALF]), ALU.mult)
                ins.then_inc(rot_ok, 1)

            def minimum(u, p):
                dve.wait_ge(s_ok, u + 1)
                if past(u, 2):
                    dve.wait_ge(exp_ok, u - 1)
                dve.tensor_reduce(nmax[:, p, :], S[:, 0, :].rearrange("p (h k) -> p h k", h=4), AX.X, ALU.min)\
                   .then_inc(min_ok, 1)

            def scale(u, p):
                dve.wait_ge(exp_ok, u + 1)
                dve.reciprocal(rsum[:, p, :], sums[:, p, :]).then_inc(pchain, 1)
                dve.wait_ge(pchain, u + 1)
                dve.tensor_tensor(prob[:, p], prob[:, p], rsum[:, p, :, None].to_broadcast([P, 4, P]),
                                  ALU.mult).then_inc(p_ok, 1)

            def evac_prob(u, p):
                dve.wait_ge(turn_ok, u + 1)
                if past(u, 2):
                    dve.wait_ge(o_ok, u - 1)
                dve.tensor_copy(probT[:, p].rearrange("p h q -> p (h q)"), PT[:, 0, :]).then_inc(probT_ok, 1)

            def concat(u, p):
                dve.wait_ge(o_ok, u + 1)
                if past(u, 2):
                    dve.wait_ge(f_ok, u - 1)
                o4 = O[:, 0, :].rearrange("p (h q) -> p h q", h=4)
                if not cross:
                    dve.tensor_copy(cat[:, p], o4).then_inc(cat_ok, 1)
                    return
                n = [0]

                def then(ins):
                    n[0] += 1
                    ins.then_inc(qchain, 1)
                    dve.wait_ge(qchain, u * 6 + n[0])
                then(dve.tensor_tensor(y[:], o4, t["smooth"][:, bass.ds(group(u) * 4, 4), None].to_broadcast([P, 4, P]),
                                       ALU.mult))
                then(dve.tensor_scalar(y[:], y[:], FP8_MAX, None, ALU.min))
                round_fp8(dve, y[:], big[:], cat[:, p], then).then_inc(cat_ok, 1)

            def accumulate(u, p):
                dve.wait_ge(f_ok, u + 1)
                to = (x if cross else t["h"])[:, batch(u), :]
                if cross:
                    dve.scalar_tensor_tensor(out=to, in0=F[:, 0, 0:D], scalar=t["proj"][:, 0:1], in1=to,
                                             op0=ALU.mult, op1=ALU.add).then_inc(acc_ok, 1)
                else:
                    dve.tensor_tensor(to, F[:, 0, 0:D], to, ALU.add).then_inc(acc_ok, 1)
            if cross:
                stages = [(0, variance), (1, minimum), (2, evac_prob), (0, normed), (3, accumulate), (1, scale),
                          (2, concat)]
            else:
                stages = [(0, rotary), (1, minimum), (2, evac_prob), (3, accumulate), (1, scale), (2, concat)]
            ticks(dve, STEPS, stages)
            if not cross:
                dve.wait_ge(acc_ok, STEPS)
                dve.tensor_tensor(x[:], x[:], t["h"][:], ALU.add)


def layer1_cross(k: Kernel):
    with ExitStack() as ctx:
        sb = lambda n, s, dt=F32: k.sb(ctx, f"c_{n}", s, dt)
        w = sb("w", [P, 8, DC, 8 * P])
        wp = sb("wp", [P, 2, 8, 4, D], BF16)
        xq = sb("xq", [P, 4, DC, T], BF16)
        smooth = sb("smooth_inv", [P, 32])
        proj = sb("proj", [P, 1])
        double_norm(k, "c", False, Quantise(xq, w, wp, {"smooth": smooth, "proj": proj}))
        ctxT = sb("ctxT2", [P, DC, B, P])
        attention(k, CrossForm, {"w": w, "wp": wp, "xq": xq, "smooth": smooth, "proj": proj, "ctxT": ctxT})


def layer1_causal(k: Kernel, h):
    with ExitStack() as ctx:
        sb = lambda n, s, dt=F32: k.sb(ctx, f"d_{n}", s, dt)
        w = sb("w", [P, 4, DC, 6 * P])
        wo = sb("wo", [P, 4, 4, D])
        nT = sb("nT", [P, DC, T])
        double_norm(k, "d", True, Keep(nT, h))
        attention(k, CausalForm, {"w": w, "wo": wo, "nT": nT, "h": h})


def program(nc, io, out):
    with ExitStack() as ctx:
        k = Kernel(nc, ctx, io)
        layer0_attention(k)
        moe(k, Moe("b", experts=16, hidden=256, topk=4, clipped=True), k.x)
        layer1_cross(k)
        h = k.sb(ctx, "h", [P, B, D])
        layer1_causal(k, h)
        moe(k, Moe("e", experts=8, hidden=512, topk=2, clipped=False), h)
        with k.nc.semaphore("y_out") as y_out, nc.Block() as block:
            @block.sync
            def _(sp):
                sp.dma_start(out, k.x[:]).then_inc(y_out, 16)
                sp.wait_ge(y_out, 16)


def laid_out(inputs):
    a = {n: np.asarray(v) for n, v in inputs.items()}
    full = lambda v, n=1: np.ascontiguousarray(np.broadcast_to(v, (P, n)))
    io = {}
    io["x"] = a["x"].transpose(1, 0, 2)
    io["ctx"] = a["ctx_2048"].transpose(1, 0, 2)
    io["ctxT"] = a["ctx_2048"].reshape(B, P, DC, P).transpose(3, 2, 0, 1)
    io["gamma"] = full(a["L0_xattn_gamma"])
    heads = (np.arange(P) // 16) % 2
    io["head_mask"] = np.stack([np.where(heads == r, -0.25, 0.0) for r in range(2)], 1).astype(np.float32)
    chunked = lambda w: w.reshape(*w.shape[:-2], w.shape[-2] // P, P, w.shape[-1]).swapaxes(-3, -2)
    ones, zeros = np.ones((P, DC), np.float32), np.zeros((P, DC), np.float32)
    io["b_rw"] = chunked(a["L0_ffn_router_weight"].T)
    io["b_rb"] = full(a["L0_ffn_router_bias"], 16)
    io["b_chan"] = np.stack([ones, zeros], 2)
    io["b_db"] = a["L0_ffn_down_proj_bias"]
    gu = a["L0_ffn_gate_up_proj"].reshape(16, DC, P, 256, 2)
    io["b_w_in"] = gu.transpose(0, 2, 4, 1, 3)
    io["b_w_out"] = chunked(a["L0_ffn_down_proj"])
    io["b_bias"] = a["L0_ffn_gate_up_proj_bias"].reshape(16, 2, P, 2).transpose(0, 2, 3, 1)
    io["c_chan"] = np.stack([a["L1_xattn_ln_w"].reshape(DC, P).T, a["L1_xattn_ln_b"].reshape(DC, P).T], 2)
    by_head = lambda w, heads: w.T.reshape(DC, P, 8, heads * P).transpose(1, 2, 0, 3)
    kvx = a["L1_xattn_w_kv_x"]
    io["c_w"] = np.concatenate([by_head(a["L1_xattn_wq"], 2), by_head(a["L1_xattn_wqx"], 2), by_head(a["L1_xattn_wk"], 1),
                                by_head(kvx[:1024], 1), by_head(a["L1_xattn_wv"], 1), by_head(kvx[1024:], 1)], 3)
    io["c_wp"] = a["L1_xattn_wproj"].T.reshape(2, 8, 2, P, D).transpose(3, 1, 0, 2, 4).reshape(P, 8, 4, D)
    io["c_smooth"] = a["L1_xattn_proj_smooth"].reshape(2, 8, 2, P).transpose(3, 1, 0, 2).reshape(P, 8, 4)
    kinds = ("q", "qx", "k", "v")
    io["c_in_scale"] = np.stack([a[f"L1_xattn_{n}_in_scale"].reshape(DC, P).T for n in kinds], 1)
    io["c_w_scale"] = np.concatenate([full(a[f"L1_xattn_w{n}_scale"]) for n in kinds], 1)
    io["c_p_scale"] = np.concatenate([full(a["L1_xattn_proj_in_scale"]), full(a["L1_xattn_proj_w_scale"])], 1)
    io["c_hw"] = np.stack([np.stack([a[f"L1_xattn_{n}ln_w"], a[f"L1_xattn_{n}ln_b"]], 1) for n in ("q", "qx", "k", "kx")], 1)
    io["d_chan"] = np.stack([a["L1_ffn_norm1_w"].reshape(DC, P).T, zeros], 2)
    by_group = lambda w, heads: w.reshape(DC, P, 4, heads * P).transpose(1, 2, 0, 3)
    io["d_w"] = np.concatenate([by_group(a["L1_ffn_wq"], 4), by_group(a["L1_ffn_wk"], 1), by_group(a["L1_ffn_wv"], 1)], 3)
    io["d_wo"] = a["L1_ffn_wo"].reshape(4, 4, P, D).transpose(2, 0, 1, 3)
    freq = np.float32(1.0) / np.float32(1e6) ** (np.arange(0, P, 2, dtype=np.float32) / np.float32(P))
    angle = np.arange(P, dtype=np.float32)[:, None] * freq[None, :]
    io["d_cos"] = np.concatenate([np.cos(angle)] * 2, 1)
    io["d_sin"] = np.concatenate([-np.sin(angle), np.sin(angle)], 1)
    io["e_rw"] = chunked(a["L1_ffn_gate_w"])
    io["e_rb"] = np.zeros((P, 8), np.float32)
    io["e_chan"] = np.stack([a["L1_ffn_norm2_w"].reshape(DC, P).T, zeros], 2)
    w13 = np.stack([a["L1_ffn_w1"], a["L1_ffn_w3"]], 1).reshape(8, 2, DC, P, 512)
    io["e_w_in"] = w13.transpose(0, 3, 1, 2, 4)
    io["e_w_out"] = chunked(a["L1_ffn_w2"])
    return {n: np.ascontiguousarray(v) for n, v in io.items()}


def kernel(**inputs):
    import concourse.bacc as bacc
    from concourse.bass_utils import run_bass_kernel_spmd

    nc = bacc.Bacc("TRN2", target_bir_lowering=False, num_devices=1)
    arrays = laid_out(inputs)
    io = {n: nc.dram_tensor(f"in_{n}", v.shape, mybir.dt.from_np(v.dtype), kind="ExternalInput").ap()
          for n, v in arrays.items()}
    out = nc.dram_tensor("out_y", (P, B, D), F32, kind="ExternalOutput").ap()
    program(nc, io, out)
    r = run_bass_kernel_spmd(nc, [{f"in_{n}": v for n, v in arrays.items()}], core_ids=[0])
    return np.ascontiguousarray(r.results[0]["out_y"].transpose(1, 0, 2))
```
